# Optimizing a Trainium2 kernel written in Bass

```python
import numpy as np
import jax
import jax.numpy as jnp

def _softmax(x, axis=-1):
    return jax.nn.softmax(x, axis=axis)

def _gelu(x):
    return jax.nn.gelu(x, approximate=True)

def _silu(x):
    return jax.nn.silu(x)

def _sigmoid(x):
    return jax.nn.sigmoid(x)

def _layernorm(x, axis=-1, eps=1e-05):
    m = jnp.mean(x, axis=axis, keepdims=True)
    v = jnp.var(x, axis=axis, keepdims=True)
    return (x - m) / jnp.sqrt(v + eps)

def _scatter_add(tgt, idx, src, axis=0):
    return tgt.at[idx].add(src)

def _segment_sum(src, seg, n):
    return jax.ops.segment_sum(src, seg, n)
kernel_name = 'mk_sandwich_d1_jaxref_r4_b61a87'

def setup_inputs(seed: int=0):
    np.random.seed(seed)
    _w = jnp.asarray

    def _L0_attn_setup():
        import jax, jax.numpy as jnp
        import numpy as np
        N_IN = 256
        KSIZE = 31
        PAD_L = 30
        HEADS = 16
        key = jax.random.key(seed)
        k1, k2 = jax.random.split(key)
        B, T, C = (2, 512, N_IN)
        x = jax.random.normal(k1, (B, T, C), dtype=jnp.float32)
        w_lin = jax.random.normal(k2, (HEADS * KSIZE, C), dtype=jnp.float32) * (1.0 / np.sqrt(C))
        return {'x': x, 'w_lin': w_lin}
    _L0_attn_in = _L0_attn_setup()

    def _L0_ffn_setup():
        import jax, jax.numpy as jnp
        import numpy as np
        HIDDEN = 256
        MOE_FF = 128
        SHARED_FF = 704
        NUM_EXPERTS = 16
        TOP_K = 2
        NORM_TOPK = True
        key = jax.random.key(seed)
        ks = jax.random.split(key, 8)
        s = 0.02
        return {'layer_input': jax.random.normal(ks[0], (1, 512, HIDDEN), dtype=jnp.float32), 'gate_w': jax.random.normal(ks[1], (NUM_EXPERTS, HIDDEN), dtype=jnp.float32) * s, 'w_gate_up': jax.random.normal(ks[2], (NUM_EXPERTS, HIDDEN, 2 * MOE_FF), dtype=jnp.float32) * s, 'w_down': jax.random.normal(ks[3], (NUM_EXPERTS, MOE_FF, HIDDEN), dtype=jnp.float32) * s, 'shared_w_gate': jax.random.normal(ks[4], (SHARED_FF, HIDDEN), dtype=jnp.float32) * s, 'shared_w_up': jax.random.normal(ks[5], (SHARED_FF, HIDDEN), dtype=jnp.float32) * s, 'shared_w_down': jax.random.normal(ks[6], (HIDDEN, SHARED_FF), dtype=jnp.float32) * s, 'shared_gate_w': jax.random.normal(ks[7], (1, HIDDEN), dtype=jnp.float32) * s}
    _L0_ffn_in = _L0_ffn_setup()
    _d = {'L0_attn_x': _L0_attn_in['x'], 'L0_attn_w_lin': _L0_attn_in['w_lin'], 'L0_ffn_gate_w': _L0_ffn_in['gate_w'], 'L0_ffn_w_gate_up': _L0_ffn_in['w_gate_up'], 'L0_ffn_w_down': _L0_ffn_in['w_down'], 'L0_ffn_shared_w_gate': _L0_ffn_in['shared_w_gate'], 'L0_ffn_shared_w_up': _L0_ffn_in['shared_w_up'], 'L0_ffn_shared_w_down': _L0_ffn_in['shared_w_down'], 'L0_ffn_shared_gate_w': _L0_ffn_in['shared_gate_w']}
    _x0 = _d['L0_attn_x']
    _d['L0_attn_x'] = jax.random.normal(jax.random.fold_in(jax.random.key(seed), 1), (4, 2048, 256), dtype=_x0.dtype)
    del _x0
    return _d

def reference(L0_attn_x, L0_attn_w_lin, L0_ffn_gate_w, L0_ffn_w_gate_up, L0_ffn_w_down, L0_ffn_shared_w_gate, L0_ffn_shared_w_up, L0_ffn_shared_w_down, L0_ffn_shared_gate_w):

    def _L0_attn_ref(x, w_lin):
        import jax, jax.numpy as jnp
        import numpy as np
        N_IN = 256
        KSIZE = 31
        PAD_L = 30
        HEADS = 16
        B, T, C = x.shape
        H, K, P = (HEADS, KSIZE, PAD_L)
        R = C // H
        w = jnp.einsum('btc,fc->btf', x, w_lin).reshape(B, T, H, K)
        w = jax.nn.softmax(w.astype(jnp.float32), axis=-1).astype(x.dtype)
        w = w.transpose(0, 2, 1, 3)
        t_idx = jnp.arange(T)[:, None]
        s_idx = jnp.arange(T)[None, :]
        kidx = s_idx - t_idx + P
        mask = (kidx >= 0) & (kidx < K)
        kidx_c = jnp.clip(kidx, 0, K - 1)
        we = jnp.take_along_axis(w, jnp.broadcast_to(kidx_c, (B, H, T, T)), axis=-1)
        we = jnp.where(mask, we, jnp.zeros((), dtype=we.dtype))
        xh = x.reshape(B, T, H, R).transpose(0, 2, 1, 3)
        out = jnp.einsum('bhts,bhsr->bhtr', we, xh)
        return out.transpose(0, 2, 1, 3).reshape(B, T, C)

    def _L0_ffn_ref(layer_input, gate_w, w_gate_up, w_down, shared_w_gate, shared_w_up, shared_w_down, shared_gate_w):
        import jax, jax.numpy as jnp
        import numpy as np
        HIDDEN = 256
        MOE_FF = 128
        SHARED_FF = 704
        NUM_EXPERTS = 16
        TOP_K = 2
        NORM_TOPK = True
        B, S, D = layer_input.shape
        x = layer_input.reshape(-1, D)
        N = x.shape[0]
        shared = jax.nn.silu(x @ shared_w_gate.T) * (x @ shared_w_up.T) @ shared_w_down.T
        shared = shared * jax.nn.sigmoid(x @ shared_gate_w.T)
        logits = x @ gate_w.T
        probs = jax.nn.softmax(logits.astype(jnp.float32), axis=-1)
        rw, sel = jax.lax.top_k(probs, TOP_K)
        if NORM_TOPK:
            rw = rw / rw.sum(axis=-1, keepdims=True)
        rw = rw.astype(x.dtype)
        combine = jnp.zeros((N, NUM_EXPERTS), x.dtype).at[jnp.arange(N)[:, None], sel].set(rw)
        gu = jnp.einsum('nd,edf->nef', x, w_gate_up)
        g, h = jnp.split(gu, 2, axis=-1)
        h = jax.nn.silu(g) * h
        expert_out = jnp.einsum('nef,efd,ne->nd', h, w_down, combine)
        out = expert_out + shared
        return out.reshape(B, S, D)
    x = L0_attn_x
    x = x + _layernorm(_L0_attn_ref(_layernorm(x, axis=-1), L0_attn_w_lin), axis=-1)
    x = x + _layernorm(_L0_ffn_ref(_layernorm(x, axis=-1), L0_ffn_gate_w, L0_ffn_w_gate_up, L0_ffn_w_down, L0_ffn_shared_w_gate, L0_ffn_shared_w_up, L0_ffn_shared_w_down, L0_ffn_shared_gate_w), axis=-1)
    return x

_drawn_inputs = setup_inputs


def setup_inputs(seed=0):
    import zlib

    import numpy as np

    out = dict(_drawn_inputs(seed))
    spreads = {}
    factors = {}
    for name, (base, spread) in spreads.items():
        noise = np.random.default_rng([zlib.crc32(name.encode()), seed]).standard_normal(out[name].shape)
        drawn = base * np.exp(spread * noise) if base else spread * noise
        out[name] = jnp.asarray(drawn.astype(out[name].dtype))
    for name, factor in factors.items():
        out[name] = (out[name] * factor).astype(out[name].dtype)
    return out
```

```python
from contextlib import ExitStack

import concourse.bass as bass
from concourse import mybir

F32 = mybir.dt.float32
F32R = mybir.dt.float32r
U32 = mybir.dt.uint32
I32 = mybir.dt.int32
ALU = mybir.AluOpType
ACT = mybir.ActivationFunctionType
AX = mybir.AxisListType

P = 128
BATCH, SEQ, C = 4, 2048, 256
T = BATCH * SEQ
HEADS, KS, HC = 16, 31, 16
CC = C // P
J = 32
HALVES = 2
NB = T // J // HALVES
NBB = SEQ // J
HS, NG = 4, 4
SLOT_C = C // HS
MW = SLOT_C + HS
CB = 8
NCH = NB // CB
NT = T // P
FF, E, MF = 704, 16, 128
FT = 6
FL = FF - (FT - 1) * P
GW = 18
TOPK = 2
NBLK = T * TOPK // P + E - 1
SLOTS = (NBLK + 1) * P
SPARE = NBLK + 1 + E
PACK, PACK_BITS = 5, 4
EPS = 1e-5
CONSTS = 8 + 4 * HS


def wait_apart(eng, passed, sem, value):
    eng.wait_ge(sem, value)
    eng.sem_inc(passed, 1)


def build_program(nc, x, wd, gw, wsh, wdn, we, out):
    first_d = nc.dram_tensor("first_stores", [32, P, 4], F32).ap()
    xn_d = nc.dram_tensor("xn_scratch", [BATCH, NBB + 1, J, C], F32).ap()
    yn_d = nc.dram_tensor("yn_scratch", [NT, P, C], F32).ap()
    ynt_d = nc.dram_tensor("ynt_scratch", [NT, P, CC, P], F32).ap()
    x2_d = nc.dram_tensor("x2_scratch", [NT, P, C], F32).ap()
    sh_d = nc.dram_tensor("shared_scratch", [NT // 2, P, C], F32).ap()
    xg_d = nc.dram_tensor("sorted_rows", [(SPARE + E) * P, C], F32).ap()
    yg_d = nc.dram_tensor("expert_rows", [SLOTS, C], F32).ap()

    with ExitStack() as ctx:
        def sb(name, shape, dt=F32):
            return ctx.enter_context(nc.sbuf_tensor(name, shape, dt))

        ident = sb("ident", [P, P])
        ones = sb("ones", [P, P])
        neg_half = sb("neg_half", [P, 2])
        eps = sb("eps", [P, 2])
        logits = sb("logits", [P, NT, GW])
        slots = sb("slots", [P, NT, TOPK], U32)
        share = sb("share", [P, NT, TOPK])
        shgate = sb("shgate", [P, NT])
        no_row = sb("no_row", [P, C])
        block_expert = sb("block_expert", [1, NBLK + 1 + PACK], I32)
        pb = [ctx.enter_context(nc.psum_tensor(f"bank{i}", [P, 512], F32)) for i in range(8)]
        top = TopTwo(nc, logits, sb, ctx.enter_context(nc.semaphore("top_step")))
        attention(nc, x, wd, gw, first_d, xn_d, yn_d, ynt_d, x2_d, ident, ones, neg_half, eps, logits, top, pb)
        sems = {n: ctx.enter_context(nc.semaphore("sh_" + n)) for n in Shared.SEMS}
        yt = sb("yt", [P, 2, 4, CC, P])
        cleared = ctx.enter_context(nc.semaphore("cleared"))
        split = [sb(name, shape, F32R) for name, shape in
                 (("gh", [P, CC, 2 * FF]), ("gl", [P, CC, 2 * FF]), ("dh", [P, FT, C]), ("dl", [P, FT, C]))]
        routing(nc, logits, slots, share, shgate, block_expert, no_row, xg_d, cleared, sems, yt, ynt_d, ident, ones,
                wsh, wdn, split, top, pb)
        with ExitStack() as inner:
            eh = inner.enter_context(nc.sbuf_tensor("eh", [P, E, 3 * C], F32R))
            el = inner.enter_context(nc.sbuf_tensor("el", [P, E, 3 * C], F32R))
            shared_and_scatter(nc, sems, we, split, eh, el, yt, ynt_d, yn_d, xg_d, first_d, slots, shgate, sh_d, cleared, pb)
            experts(nc, sems, eh, el, yt, ynt_d, first_d, xg_d, yg_d, ident, ones, block_expert, pb)
        shared_and_combine(nc, sems, split, yt, first_d, ynt_d, x2_d, yg_d, sh_d, ones, neg_half, eps, slots, share, shgate, out, pb)


class TopTwo:

    EARLY = NT - 8

    def __init__(self, nc, logits, sb, s_step):
        self.nc, self.logits, self.s_step, self.steps = nc, logits, s_step, 0
        self.iota = sb("iota_i", [P, E], I32)
        self.rev = sb("rev", [P, E])
        self.best = sb("best", [P, TOPK, NT])
        self.which = sb("which", [P, TOPK, NT])

    def done(self, ve, ins):
        self.steps += 1
        ins.then_inc(self.s_step, 1)
        ve.wait_ge(self.s_step, self.steps)

    @staticmethod
    def over_experts(t, n):
        return t[:, :, None].to_broadcast([P, n, E])

    def find(self, ve, lo, hi, pick, rest):
        v, n = self.nc.vector, hi - lo
        lg = self.logits[:, lo:hi, 0:E]
        rv = self.rev[:, None, :].to_broadcast([P, n, E])
        for k in range(TOPK):
            src = lg if k == 0 else rest[:]
            best, which = self.best[:, k, lo:hi], self.which[:, k, lo:hi]
            self.done(ve, v.tensor_reduce(best, src, AX.X, ALU.max))
            self.done(ve, v.tensor_tensor(pick[:], src, self.over_experts(best, n), ALU.is_equal))
            self.done(ve, v.tensor_tensor(pick[:], pick[:], rv, ALU.mult))
            self.done(ve, v.tensor_reduce(which, pick[:], AX.X, ALU.max))
            if k == 0:
                self.done(ve, v.tensor_tensor(pick[:], rv, self.over_experts(which, n), ALU.is_equal))
                self.done(ve, v.scalar_tensor_tensor(rest[:], pick[:], -3e38, lg, ALU.mult, ALU.add))


def skewed(eng, count, *work):
    lead, lag = max(0, *(o for o, _ in work)), max(0, *(-o for o, _ in work))

    def step(i, q):
        for offset, f in work:
            if not isinstance(i, int) or 0 <= i + offset < count:
                f(i + offset, (q + offset) % 2)

    U = 4 if count - lead - lag >= 8 else 2
    turns = (count - lead - lag) // U
    for i in range(-lead, lag):
        step(i, i % 2)
    with eng.Fori(0, turns) as k:
        for u in range(U):
            step(k * U + (lag + u), (lag + u) % 2)
    for i in range(lag + U * turns, count + lag):
        step(i, i % 2)


def attention(nc, x, wd, gw, first_d, xn_d, yn_d, ynt_d, x2_d, ident, ones, neg_half, eps, logits, top, pb):
    x_blk = x.rearrange("(h u) (b j) c -> h (u b) j c", h=HALVES, j=J)
    x_nat = x.rearrange("a (n p) c -> (a n) p c", p=P)

    with ExitStack() as ctx:
        def sb(name, shape, dt=F32):
            return ctx.enter_context(nc.sbuf_tensor(name, shape, dt))

        def sem(name):
            return ctx.enter_context(nc.semaphore(name))

        wraw = sb("wraw", [P, CC, HEADS, 64])
        wh = sb("wh", [P, CC, HEADS, 64], F32R)
        wl = sb("wl", [P, CC, HEADS, 64], F32R)
        xt = sb("xt", [P, 2, 2, C])
        xn = sb("xn", [P, 2, 2, C])
        st = sb("st", [P, 2, 2, 6])
        mv = sb("mv", [P, 2, 2, 2])
        rstd = sb("rstd", [P, 2, 2])
        shift = sb("shift", [P, 2, 2])
        xth = sb("xth", [P, 2, 2, C], F32R)
        xtl = sb("xtl", [P, 2, 2, C], F32R)
        mx = sb("mx", [P, 2, 2, HEADS])
        ew = sb("ew", [P, 2, 2, NG, HS, J])
        probs = sb("probs", [P, NB, NG, J])
        xs = sb("xs", [P, 2, CB + 1, SLOT_C])
        xbd = sb("xbd", [P, 2, CB + 1, NG, MW])
        am = sb("am", [P, 2, NG, CB, 2, J])
        mask = sb("mask", [P, 2, J])
        ot = sb("ot", [P, 2, NG, CB * J])
        xr = sb("xr", [P, 2, 2, C])
        rs = sb("rs", [P, 2, HEADS])
        av = sb("av", [P, 2, 2, C])
        st2 = sb("st2", [P, 2, 2, 6])
        mv2 = sb("mv2", [P, 2, 2, 2])
        rstd2 = sb("rstd2", [P, 2, 2])
        shift2 = sb("shift2", [P, 2, 2])
        x2 = sb("x2", [P, 2, 2, C])
        st3 = sb("st3", [P, 2, 2, 6])
        mv3 = sb("mv3", [P, 2, 2, 2])
        rstd3 = sb("rstd3", [P, 2, 2])
        shift3 = sb("shift3", [P, 2, 2])
        yn = sb("yn", [P, 2, 2, C])
        ynt = sb("ynt", [P, 2, 2, CC, P])
        gws = sb("gws", [P, CC, GW])
        pick = sb("a_pick", [P, top.EARLY, E])
        rest = sb("a_rest", [P, top.EARLY, E])
        zero = sb("zero", [P, C])
        names = """ve_passed sp_passed w_in w_hi w_lo zeros consts gw_in padded
            x_in0 x_in1 st_ok mv_ok var_ok dev_ok norm_ok xn_ok xn_out0 xn_out1
            psx_full xth_ok xtl_ok psl_full mx_ok sub_ok exp_ok pse_full probs_ok
            xs_in0 xs_in1 xbd_ok am_ok pso_full ot_ok psb_full rs_ok av_ok st2_ok mv2_ok var2_ok dev2_ok norm2_ok
            z_ok xr_in0 xr_in1 x2_ok st3_ok mv3_ok var3_ok dev3_ok norm3_ok yn_ok psy_full ynt_ok psg_full lg_ok
            x2_out0 x2_out1 yn_out0 yn_out1 ynt_out0 ynt_out1""".split()
        s = {n: sem(n) for n in names}
        block = ctx.enter_context(nc.Block())

        psx, psl, pse = pb[0:2], (pb[2:4], pb[4:6]), pb[6:8]
        pso, psb, psy = (pb[0:2], pb[2:4]), pb[4:6], pb[6:8]
        NPR = J // 2
        xn_rows = xn_d.rearrange("a b j c -> (a b) j c")


        @block.sync
        def _(sp):
            sp.dma_start(wraw[:], wd).then_inc(s["w_in"], 16)
            sp.dma_start(gws[:], gw).then_inc(s["gw_in"], 16)
            with sp.Fori(0, HALVES) as h:
                def load_x(i, q):
                    sp.wait_ge(s["xn_ok"], (h * NPR + i) * 2 + 2)
                    sp.dma_start(xt[:, q], x_blk[h, :, bass.ds(i * 2, 2), :]).then_inc(s[f"x_in{q}"], 16)

                def store_xn(i, q):
                    sp.wait_ge(s["xn_ok"], (h * NPR + i) * 2 + 6)
                    for u in range(2):
                        sp.dma_start(xn_d[h * 2 + u, 1:, bass.ds(i * 2, 2), :],
                                     xn[64 * u:64 * u + 64, q]).then_inc(s[f"xn_out{q}"], 16)

                skewed(sp, NPR, (4, load_x), (2, store_xn))
                sp.wait_ge(s["zeros"], 1)
                for u in range(2):
                    sp.dma_start(xn_d[h * 2 + u, 0], zero[0:J, 0:C]).then_inc(s["padded"], 16)
                wait_apart(sp, s["sp_passed"], s["padded"], (h + 1) * 32)
                for q in range(2):
                    wait_apart(sp, s["sp_passed"], s[f"xn_out{q}"], (h + 1) * (NPR * 16) + 16)

                def load_xs(i, q):
                    n = h * NCH + i
                    sp.wait_ge(s["xbd_ok"], n + 1)
                    start = h * (2 * (NBB + 1)) + i * CB + i // (NCH // 2)
                    for k in range(HS):
                        sp.dma_start(xs[32 * k:32 * k + 32, q],
                                     xn_rows[bass.ds(start, CB + 1), :, k * SLOT_C:(k + 1) * SLOT_C].rearrange("b j c -> j b c")
                                     ).then_inc(s[f"xs_in{q}"], 16)

                def load_xr(i, q):
                    n = h * NCH + i
                    sp.wait_ge(s["x2_ok"], n * 2 + 2)
                    sp.dma_start(xr[:, q], x_nat[bass.ds(n * 2, 2)].rearrange("t p c -> p t c")).then_inc(s[f"xr_in{q}"], 16)

                def store_x2(i, q):
                    n = h * NCH + i
                    sp.wait_ge(s["x2_ok"], n * 2 + 6)
                    sp.dma_start(x2_d[bass.ds(n * 2, 2)].rearrange("t p c -> p t c"), x2[:, q]).then_inc(s[f"x2_out{q}"], 16)

                def store_yn(i, q):
                    n = h * NCH + i
                    sp.wait_ge(s["yn_ok"], n * 2 + 6)
                    sp.dma_start(yn_d[bass.ds(n * 2, 2)].rearrange("t p c -> p t c"), yn[:, q]).then_inc(s[f"yn_out{q}"], 16)

                def store_ynt(i, q):
                    n = h * NCH + i
                    sp.wait_ge(s["ynt_ok"], n * 2 + 2)
                    sp.dma_start(ynt_d[bass.ds(n * 2, 2)].rearrange("n p c t -> p n c t"), ynt[:, q]).then_inc(s[f"ynt_out{q}"], 16)

                skewed(sp, NCH, (2, load_xs), (-1, load_xr), (-2, store_x2), (-3, store_yn), (-4, store_ynt))
            for q in range(2):
                for name in ("x2_out", "yn_out", "ynt_out"):
                    sp.wait_ge(s[f"{name}{q}"], HALVES * NCH * 8 + 16)

        @block.gpsimd
        def _(po):
            nc.gpsimd.memset(zero[:], 0.0).then_inc(s["zeros"], 1)
            nc.gpsimd.memset(ident[:], 0.0).then_inc(s["consts"], 1)
            nc.gpsimd.memset(ones[:], 1.0).then_inc(s["consts"], 1)
            nc.gpsimd.memset(neg_half[:], -0.5).then_inc(s["consts"], 1)
            nc.gpsimd.memset(eps[:], EPS).then_inc(s["consts"], 1)
            nc.gpsimd.memset(xbd[:], 0.0).then_inc(s["consts"], 1)
            nc.gpsimd.memset(mask[:], 1.0).then_inc(s["consts"], 1)
            nc.gpsimd.iota(top.iota[:], pattern=[[-1, E]], base=E, channel_multiplier=0).then_inc(s["consts"], 1)
            po.wait_ge(s["zeros"], 1)
            po.wait_ge(s["consts"], 7)
            nc.gpsimd.affine_select(out=ident[:], in_=ident[:], compare_op=ALU.not_equal, fill=1.0, base=0,
                                    pattern=[[-1, P]], channel_multiplier=1).then_inc(s["consts"], 1)
            done = 8
            for k in range(HS):
                part = slice(32 * k, 32 * k + 32)
                po.wait_ge(s["consts"], done)
                nc.gpsimd.memset(xbd[part, :, :, :, SLOT_C + k:SLOT_C + k + 1], 1.0).then_inc(s["consts"], 1)
                nc.gpsimd.affine_select(out=mask[part, 0], in_=mask[part, 0], compare_op=ALU.is_ge, fill=0.0, base=-2,
                                        pattern=[[-1, J]], channel_multiplier=1).then_inc(s["consts"], 1)
                nc.gpsimd.affine_select(out=mask[part, 1], in_=mask[part, 1], compare_op=ALU.is_ge, fill=0.0, base=0,
                                        pattern=[[1, J]], channel_multiplier=-1).then_inc(s["consts"], 1)
                done += 3
                po.wait_ge(s["consts"], done)
                nc.gpsimd.affine_select(out=mask[part, 1], in_=mask[part, 1], compare_op=ALU.is_ge, fill=0.0, base=J - 2,
                                        pattern=[[-1, J]], channel_multiplier=1).then_inc(s["consts"], 1)
                done += 1
            po.wait_ge(s["consts"], CONSTS)

            def scales(n, q, mv_, rstd_, shift_, k):
                po.wait_ge(s[f"mv{k}_ok"], n * 2 + 2)
                nc.gpsimd.tensor_tensor(rstd_[:, q], mv_[:, q, :, 1], eps[:, 0:2], ALU.add).then_inc(s[f"var{k}_ok"], 1)
                nc.gpsimd.tensor_tensor(shift_[:, q], zero[:, 0:2], mv_[:, q, :, 0], ALU.subtract).then_inc(s[f"var{k}_ok"], 1)
                po.wait_ge(s[f"var{k}_ok"], n * 2 + 2)
                nc.gpsimd.tensor_tensor(rstd_[:, q], rstd_[:, q], neg_half[:, 0:2], ALU.pow).then_inc(s[f"dev{k}_ok"], 1)
                po.wait_ge(s[f"dev{k}_ok"], n + 1)
                nc.gpsimd.tensor_tensor(shift_[:, q], shift_[:, q], rstd_[:, q], ALU.mult).then_inc(s[f"norm{k}_ok"], 1)

            po.sem_inc(s["x2_ok"], 4)
            with po.Fori(0, HALVES) as h:
                def residual(i, q):
                    n = h * NCH + i
                    po.wait_ge(s[f"xr_in{q}"], (n - q) * 8 + 16)
                    po.wait_ge(s[f"x2_out{q}"], (n - q) * 8 + 16)
                    po.wait_ge(s["yn_ok"], n * 2 + 2)
                    for t in range(2):
                        po.wait_ge(s["z_ok"], n * 2 + t + 1)
                        nc.gpsimd.tensor_tensor(x2[:, q, t], av[:, q, t], xr[:, q, t], ALU.add).then_inc(s["x2_ok"], 1)

                skewed(po, NPR, (3, lambda i, q: scales(h * NPR + i, q, mv, rstd, shift, "")))
                skewed(po, NCH, (-2, residual), (-1, lambda i, q: scales(h * NCH + i, q, mv2, rstd2, shift2, 2)),
                       (-2, lambda i, q: scales(h * NCH + i, q, mv3, rstd3, shift3, 3)))

        @block.vector
        def _(ve):
            for name, places in (("xtl_ok", 2), ("sub_ok", 4), ("av_ok", 2)):
                ve.sem_inc(s[name], places)
            ve.wait_ge(s["w_hi"], 1)
            nc.vector.tensor_tensor(wl[:], wraw[:], wh[:].bitcast(F32), ALU.subtract).then_inc(s["w_lo"], 1)
            with ve.Fori(0, HALVES) as h:
                def spread(i, q):
                    for u in range(2):
                        m = (h * NPR + i) * 2 + u
                        ve.wait_ge(s["psl_full"], m + 5)
                        nc.vector.tensor_reduce(mx[:, q, u], psl[q][u][:].rearrange("p (h r) -> p h r", r=J), AX.X, ALU.max
                                                ).then_inc(s["mx_ok"], 1)
                    for u in range(2):
                        m = (h * NPR + i) * 2 + u
                        ve.wait_ge(s["mx_ok"], m + 1)
                        ve.wait_ge(s["pse_full"], m + 1)
                        nc.vector.tensor_tensor(
                            ew[:, q, u].rearrange("p g k r -> p k g r"),
                            psl[q][u][:].rearrange("p (k g r) -> p k g r", k=HS, g=NG),
                            mx[:, q, u].rearrange("p (k g) -> p k g", k=HS)[:, :, :, None].to_broadcast([P, HS, NG, J]),
                            ALU.subtract).then_inc(s["sub_ok"], 1)

                def low(i, q):
                    for u in range(2):
                        ve.wait_ge(s["xth_ok"], (h * NPR + i) * 2 + u + 1)
                        nc.vector.tensor_tensor(xtl[:, q, u], psx[u][:, 0:C], xth[:, q, u].bitcast(F32),
                                                ALU.subtract).then_inc(s["xtl_ok"], 1)

                def moments(i, q):
                    n = h * NPR + i
                    ve.wait_ge(s[f"x_in{q}"], (n - q) * 8 + 16)
                    for u in range(2):
                        nc.vector.bn_stats(st[:, q, u], xt[:, q, u]).then_inc(s["st_ok"], 1)
                    for u in range(2):
                        wait_apart(ve, s["ve_passed"], s["st_ok"], n * 2 + u + 1)
                        nc.vector.bn_aggr(mv[:, q, u], st[:, q, u]).then_inc(s["mv_ok"], 1)

                skewed(ve, NPR, (-1, spread), (1, low), (3, moments))

                def masked(i, q):
                    n = h * NCH + i
                    ve.wait_ge(s["probs_ok"], (h + 1) * J)
                    ve.wait_ge(s["pso_full"], n + 1)
                    for g in range(NG):
                        nc.vector.tensor_tensor(
                            am[:, q, g],
                            probs[:, bass.ds(i * CB, CB), g, None, :].to_broadcast([P, CB, 2, J]),
                            mask[:, None].to_broadcast([P, CB, 2, J]), ALU.mult).then_inc(s["am_ok"], 1)

                def divided(i, q):
                    for t in range(2):
                        m = (h * NCH + i) * 2 + t
                        pv = psb[t][:, 0:NG * MW].rearrange("p (g w) -> p g w", g=NG)
                        ve.wait_ge(s["psb_full"], m + 1)
                        nc.vector.reciprocal(rs[:, t].rearrange("p (k g) -> p g k", g=NG),
                                             pv[:, :, SLOT_C:MW]).then_inc(s["rs_ok"], 1)
                        ve.wait_ge(s["rs_ok"], m + 1)
                        nc.vector.tensor_tensor(
                            av[:, q, t].rearrange("p (k g r) -> p g k r", k=HS, g=NG),
                            pv[:, :, 0:SLOT_C].rearrange("p g (k r) -> p g k r", k=HS),
                            rs[:, t].rearrange("p (k g) -> p g k", g=NG)[:, :, :, None].to_broadcast([P, NG, HS, HC]),
                            ALU.mult).then_inc(s["av_ok"], 1)
                    for t in range(2):
                        m = (h * NCH + i) * 2 + t
                        ve.wait_ge(s["av_ok"], m + 3)
                        nc.vector.bn_stats(st2[:, q, t], av[:, q, t]).then_inc(s["st2_ok"], 1)
                    for t in range(2):
                        m = (h * NCH + i) * 2 + t
                        wait_apart(ve, s["ve_passed"], s["st2_ok"], m + 1)
                        nc.vector.bn_aggr(mv2[:, q, t], st2[:, q, t]).then_inc(s["mv2_ok"], 1)

                def moments3(i, q):
                    n = h * NCH + i
                    for t in range(2):
                        ve.wait_ge(s["x2_ok"], n * 2 + t + 5)
                        nc.vector.bn_stats(st3[:, q, t], x2[:, q, t]).then_inc(s["st3_ok"], 1)
                    for t in range(2):
                        wait_apart(ve, s["ve_passed"], s["st3_ok"], n * 2 + t + 1)
                        nc.vector.bn_aggr(mv3[:, q, t], st3[:, q, t]).then_inc(s["mv3_ok"], 1)

                skewed(ve, NCH, (1, masked), (-1, divided), (-2, moments3))
            ve.wait_ge(s["consts"], CONSTS)
            top.done(ve, nc.vector.tensor_copy(top.rev[:], top.iota[:]))
            ve.wait_ge(s["lg_ok"], top.EARLY + 2)
            top.find(ve, 0, top.EARLY, pick, rest)

        @block.scalar
        def _(act):
            act.preload_act_table(ACT.Exp)
            for name, places in (("xn_ok", 4), ("xbd_ok", 2), ("yn_ok", 4), ("lg_ok", 2)):
                act.sem_inc(s[name], places)
            act.wait_ge(s["w_in"], 16)
            nc.scalar.activation(wh[:], wraw[:], ACT.Copy).then_inc(s["w_hi"], 1)
            act.wait_ge(s["zeros"], 1)
            for k, name in enumerate("xn_out0 xn_out1 x2_out0 x2_out1 yn_out0 yn_out1 ynt_out0 ynt_out1".split()):
                act.dma_start(first_d[k], zero[:, 0:4]).then_inc(s[name], 16)
            with act.Fori(0, HALVES) as h:
                def normal(i, q):
                    n = h * NPR + i
                    act.wait_ge(s["norm_ok"], n + 1)
                    act.wait_ge(s[f"xn_out{q}"], (n - q) * 16 + 16)
                    for u in range(2):
                        nc.scalar.activation(xn[:, q, u], xt[:, q, u], ACT.Identity, scale=rstd[:, q, u:u + 1],
                                             bias=shift[:, q, u:u + 1]).then_inc(s["xn_ok"], 1)

                def high(i, q):
                    for u in range(2):
                        m = (h * NPR + i) * 2 + u
                        act.wait_ge(s["psx_full"], m + 1)
                        act.wait_ge(s["psl_full"], m + 1)
                        nc.scalar.activation(xth[:, q, u], psx[u][:, 0:C], ACT.Copy).then_inc(s["xth_ok"], 1)

                def exps(i, q):
                    for u in range(2):
                        act.wait_ge(s["sub_ok"], (h * NPR + i) * 2 + u + 5)
                        nc.scalar.activation(ew[:, q, u], ew[:, q, u], ACT.Exp).then_inc(s["exp_ok"], 1)

                def keep(i, q):
                    for u in range(2):
                        act.wait_ge(s["pse_full"], (h * NPR + i) * 2 + u + 5)
                        nc.scalar.activation(probs[:, :, :, bass.ds(i * 2 + u, 1)].rearrange("p b g j -> p g b j"),
                                             pse[u][:].rearrange("p (g b j) -> p g b j", g=NG, j=1),
                                             ACT.Copy).then_inc(s["probs_ok"], 1)

                skewed(act, NPR, (-2, keep), (1, high), (-1, exps), (2, normal))

                def put_logits(i, q):
                    for t in range(2):
                        m = (h * NCH + i) * 2 + t
                        act.wait_ge(s["psg_full"], m + 1)
                        nc.scalar.activation(logits[:, bass.ds(m, 1), :], psy[t][:, None, C:C + GW], ACT.Copy).then_inc(s["lg_ok"], 1)

                def centred(i, q):
                    act.wait_ge(s["norm2_ok"], h * NCH + i + 1)
                    for t in range(2):
                        nc.scalar.activation(av[:, q, t], av[:, q, t], ACT.Identity, scale=rstd2[:, q, t:t + 1],
                                             bias=shift2[:, q, t:t + 1]).then_inc(s["z_ok"], 1)

                def normal2(i, q):
                    n = h * NCH + i
                    act.wait_ge(s["norm3_ok"], n + 1)
                    act.wait_ge(s[f"yn_out{q}"], (n - q) * 8 + 16)
                    for t in range(2):
                        nc.scalar.activation(yn[:, q, t], x2[:, q, t], ACT.Identity, scale=rstd3[:, q, t:t + 1],
                                             bias=shift3[:, q, t:t + 1]).then_inc(s["yn_ok"], 1)

                def expand(i, q):
                    n = h * NCH + i
                    act.wait_ge(s[f"xs_in{q}"], (n - q) * (8 * HS) + 16 * HS)
                    act.wait_ge(s["pso_full"], n + 1)
                    for k in range(HS):
                        part = slice(32 * k, 32 * k + 32)
                        ins = nc.scalar.activation(xbd[part, q, :, :, 16 * k:16 * k + 16],
                                                   xs[part, q].rearrange("p b (g r) -> p b g r", g=NG), ACT.Copy)
                    ins.then_inc(s["xbd_ok"], 1)

                def turned(i, q):
                    n = h * NCH + i
                    act.wait_ge(s[f"ynt_out{q}"], (n - q) * 8 + 16)
                    for t in range(2):
                        act.wait_ge(s["psy_full"], n * 2 + t + 1)
                        nc.scalar.activation(ynt[:, q, t], psy[t][:, 0:C].rearrange("p (c t) -> p c t", c=CC), ACT.Copy
                                             ).then_inc(s["ynt_ok"], 1)

                def take(i, q):
                    n = h * NCH + i
                    for k in range(2):
                        act.wait_ge(s["pso_full"], n + 3)
                        nc.scalar.activation(ot[0:MW, q, 2 * k:2 * k + 2, :],
                                             pso[q][k][0:MW, :].rearrange("p (g t) -> p g t", g=2), ACT.Copy
                                             ).then_inc(s["ot_ok"], 1)

                skewed(act, NCH, (-5, put_logits), (1, expand), (-2, centred), (-3, normal2), (-4, turned), (0, take))

        @block.tensor
        def _(pe):
            pe.wait_ge(s["consts"], CONSTS)
            pe.wait_ge(s["w_lo"], 1)
            pe.wait_ge(s["gw_in"], 16)
            for name, places in (("psl_full", 4), ("pse_full", 4), ("pso_full", 2)):
                pe.sem_inc(s[name], places)
            with pe.Fori(0, HALVES) as h:
                def turn_x(i, q):
                    for u in range(2):
                        m = (h * NPR + i) * 2 + u
                        pe.wait_ge(s["xn_ok"], m + 5)
                        pe.wait_ge(s["xtl_ok"], m + 1)
                        for c in range(CC):
                            ins = nc.tensor.transpose(psx[u][:, c * P:(c + 1) * P], xn[:, q, u, c * P:(c + 1) * P], ident[:])
                        ins.then_inc(s["psx_full"], 1)

                def taps(i, q):
                    for u in range(2):
                        m = (h * NPR + i) * 2 + u
                        pe.wait_ge(s["xtl_ok"], m + 3)
                        pe.wait_ge(s["sub_ok"], m + 1)
                        k = 0
                        for c in range(CC):
                            for a, w in ((xth, wh), (xth, wl), (xtl, wh)):
                                ins = nc.tensor.matmul(psl[q][u][:], a[:, q, u, c * P:(c + 1) * P],
                                                       w[:, c, :, bass.ds(31 - (i * 2 + u), J)],
                                                       start=(k == 0), stop=(k == 5))
                                k += 1
                        ins.then_inc(s["psl_full"], 1)

                def turn_e(i, q):
                    for u in range(2):
                        pe.wait_ge(s["exp_ok"], (h * NPR + i) * 2 + u + 1)
                        for g in range(NG):
                            ins = nc.tensor.transpose(pse[u][:, g * P:(g + 1) * P],
                                                      ew[:, q, u, g].rearrange("p k r -> p (k r)"), ident[:])
                        ins.then_inc(s["pse_full"], 1)

                skewed(pe, NPR, (-2, turn_e), (1, turn_x), (0, taps))

                def products(i, q, k):
                    n = h * NCH + i
                    pe.wait_ge(s["xbd_ok"], n + 3)
                    pe.wait_ge(s["am_ok"], (n + 1) * NG)
                    for g in (2 * k, 2 * k + 1):
                        o = pso[q][k][0:MW, (g % 2) * CB * J:(g % 2 + 1) * CB * J]
                        mov = am[:, q, g].rearrange("p b s j -> p (b s j)")
                        for b in range(-1, CB):
                            lo, hi = max(b, 0) * J, min(b + 2, CB) * J
                            m0 = 64 * b + 32 if b >= 0 else 0
                            ins = nc.tensor.matmul(o[:, lo:hi], xbd[:, q, b + 1, g, :], mov[:, m0:m0 + hi - lo],
                                                   start=(g % 2 == 0 and b < 0), stop=(g % 2 == 1 and b == CB - 1),
                                                   skip_group_check=True)
                    if k == 1:
                        ins.then_inc(s["pso_full"], 1)

                def turn_out(i, q):
                    n = h * NCH + i
                    pe.wait_ge(s["ot_ok"], n * 2 + 2)
                    for t in range(2):
                        pe.wait_ge(s["av_ok"], n * 2 + t + 1)
                        for g in range(NG):
                            ins = nc.tensor.transpose(psb[t][:, g * MW:(g + 1) * MW], ot[0:MW, q, g, t * P:(t + 1) * P],
                                                      ident[0:MW, 0:MW])
                        ins.then_inc(s["psb_full"], 1)

                def turn_yn(i, q):
                    for t in range(2):
                        m = (h * NCH + i) * 2 + t
                        pe.wait_ge(s["yn_ok"], m + 5)
                        pe.wait_ge(s["lg_ok"], m + 1)
                        for c in range(CC):
                            ins = nc.tensor.transpose(psy[t][:, c * P:(c + 1) * P], yn[:, q, t, c * P:(c + 1) * P], ident[:])
                        ins.then_inc(s["psy_full"], 1)

                def router(i, q):
                    for t in range(2):
                        pe.wait_ge(s["ynt_ok"], (h * NCH + i) * 2 + t + 1)
                        for c in range(CC):
                            ins = nc.tensor.matmul(psy[t][:, C:C + GW], ynt[:, q, t, c], gws[:, c, :],
                                                   start=(c == 0), stop=(c == CC - 1))
                        ins.then_inc(s["psg_full"], 1)

                skewed(pe, NCH, (0, lambda i, q: products(i, q, 0)), (-1, turn_out), (-4, turn_yn),
                       (0, lambda i, q: products(i, q, 1)), (-4, router))


def routing(nc, logits, slots, share, shgate, block_expert, no_row, xg_d, cleared, sems, yt, ynt_d, ident, ones, wsh, wdn, split, top, pb):
    with ExitStack() as ctx:
        def sb(name, shape, dt=F32):
            return ctx.enter_context(nc.sbuf_tensor(name, shape, dt))

        def sem(name):
            return ctx.enter_context(nc.semaphore(name))

        NBK = NBLK + 1
        rev, best = top.rev, top.best
        pick = sb("pick", [P, NT - top.EARLY, E])
        rest = sb("rest", [P, NT - top.EARLY, E])
        hot = sb("hot", [P, TOPK, NT, E])
        below = sb("below", [P, P])
        below_r = sb("below_r", [P, P], F32R)
        ones_r = sb("ones_r", [P, P], F32R)
        NBT = -(-NBK // P)
        blk_i = sb("blk_i", [P, NBT], I32)
        blk = sb("blk", [P, NBT])
        both = sb("both", [P, NT, E], F32R)
        gap = sb("gap", [P, NT])
        den = sb("den", [P, NT])
        zs = sb("zs", [P, NT])
        cs = sb("cs", [P, E, NT])
        ones_l = sb("ones_l", [P, E, NT])
        upto = sb("upto", [P, E, NT])
        edge = sb("edge", [P, E + 1])
        cnt = sb("cnt", [P, E])
        nblk = sb("nblk", [P, E])
        cblk = sb("cblk", [P, E])
        base = sb("base", [P, E])
        pos = sb("pos", [P, NT, E])
        at = sb("at", [P, TOPK, NT, E])
        slot_f = sb("slot_f", [P, TOPK, NT])
        passed = sb("passed_b", [P, NBT, E])
        bcol = sb("bcol", [P, NBT])
        clear_f = sb("clear_f", [1, E + 1])
        clear_i = sb("clear_i", [1, E + 1], I32)
        has = sb("has", [1, E])
        last = sb("last", [1, E])
        s_clear = sem("r_clear")
        bexp = sb("bexp", [1, NBK + 2 * PACK])
        packed = sb("packed", [1, NBK + PACK])

        gh, gl, dh, dl = split
        graw = sb("graw", [P, CC, 2 * FF])
        draw = sb("draw", [P, FT, C])
        s_w_in, s_split = sem("r_w_in"), sem("r_split")
        s_turn = sem("r_turn")
        s_iota, s_below, s_gap, s_exp, s_hot, s_sums = (
            sem(n) for n in "r_iota r_below r_gap r_exp r_hot r_sums".split())
        block = ctx.enter_context(nc.Block())

        def clear(eng, which):
            eng.wait_ge(s_clear, 2)
            rows = xg_d.rearrange("(b p) c -> b p c", p=P)
            for e in which:
                b = eng.value_load(clear_i[0:1, e:e + 1], min_val=0, max_val=SPARE + E - 1 if e < E else SPARE - E)
                n = 1 if e < E else E
                eng.dma_start(rows[bass.ds(b, n)].rearrange("b p c -> p b c"), no_row[:, None, :].to_broadcast([P, n, C])
                              ).then_inc(cleared, 16)

        @block.sync
        def _(sp):
            sp.dma_start(graw[:], wsh).then_inc(s_w_in, 16)
            sp.dma_start(draw[:], wdn).then_inc(s_w_in, 16)
            for n in range(2):
                load_turned(sp, sems, yt, ynt_d, n, n)
            clear(sp, range(E // 2))

        @block.gpsimd
        def _(po):
            nc.gpsimd.memset(no_row[:], 0.0).then_inc(s_clear, 1)
            nc.gpsimd.iota(blk_i[:], pattern=[[P, NBT]], base=0, channel_multiplier=1).then_inc(s_iota, 1)
            nc.gpsimd.memset(below[:], 1.0).then_inc(s_below, 1)
            nc.gpsimd.memset(ones_l[:], 1.0).then_inc(s_iota, 1)
            po.wait_ge(s_below, 1)
            nc.gpsimd.affine_select(out=below[:], in_=below[:], compare_op=ALU.is_gt, fill=0.0, base=0,
                                    pattern=[[1, P]], channel_multiplier=-1).then_inc(s_below, 1)
            po.wait_ge(s_split, 2)
            nc.gpsimd.tensor_tensor(gl[:], graw[:], gh[:].bitcast(F32), ALU.subtract)
            nc.gpsimd.tensor_tensor(dl[:], draw[:], dh[:].bitcast(F32), ALU.subtract)

        @block.scalar
        def _(act):
            act.preload_act_table(ACT.Exp)
            nc.scalar.activation(ones_r[:], ones[:], ACT.Copy)
            act.wait_ge(s_below, 2)
            nc.scalar.activation(below_r[:], below[:], ACT.Copy).then_inc(s_below, 1)
            act.wait_ge(s_gap, 1)
            nc.scalar.activation(gap[:], gap[:], ACT.Exp).then_inc(s_exp, 1)
            nc.scalar.activation(zs[:], logits[:, :, E], ACT.Exp, scale=-1.0).then_inc(s_exp, 1)
            act.wait_ge(s_w_in, 32)
            nc.scalar.activation(gh[:], graw[:], ACT.Copy).then_inc(s_split, 1)
            nc.scalar.activation(dh[:], draw[:], ACT.Copy).then_inc(s_split, 1)
            clear(act, range(E // 2, E + 1))

        @block.tensor
        def _(pe):
            pe.wait_ge(s_below, 3)
            pe.wait_ge(s_hot, 1)
            hb = both[:].rearrange("p t e -> p (t e)")
            for k in range(2):
                nc.tensor.matmul(pb[k][:], below_r[:], hb[:, 512 * k:512 * k + 512], start=True, stop=True).then_inc(s_sums, 1)
            for k in range(2):
                nc.tensor.matmul(pb[2 + k][:], ones_r[:], hb[:, 512 * k:512 * k + 512], start=True, stop=True).then_inc(s_sums, 1)
            pe.wait_ge(s_turn, 1)
            for k in range(NBT):
                ins = nc.tensor.matmul(pb[4][0:1, k * P:(k + 1) * P], bcol[:, k:k + 1], ident[:], start=True, stop=True)
            ins.then_inc(s_turn, 1)

        @block.vector
        def _(ve):
            def done(ins):
                top.done(ve, ins)

            v = nc.vector
            ve.wait_ge(s_iota, 1)
            done(v.tensor_copy(blk[:], blk_i[:]))
            done(v.memset(bexp[:, NBK:], 0.0))
            top.find(ve, top.EARLY, NT, pick, rest)
            for k in range(TOPK):
                done(v.tensor_tensor(hot[:, k], rev[:, None, :].to_broadcast([P, NT, E]),
                                     top.over_experts(top.which[:, k], NT), ALU.is_equal))
            v.tensor_tensor(both[:], hot[:, 0], hot[:, 1], ALU.add).then_inc(s_hot, 1)
            v.tensor_tensor(gap[:], best[:, 1], best[:, 0], ALU.subtract).then_inc(s_gap, 1)
            ve.wait_ge(s_exp, 2)
            done(v.tensor_scalar(den[:], gap[:], 1.0, None, ALU.add))
            done(v.reciprocal(share[:, :, 0], den[:]))
            done(v.tensor_tensor(share[:, :, 1], gap[:], share[:, :, 0], ALU.mult))
            done(v.tensor_scalar(zs[:], zs[:], 1.0, None, ALU.add))
            done(v.reciprocal(shgate[:], zs[:]))
            ve.wait_ge(s_sums, 4)
            ve.wait_ge(s_iota, 2)
            half = NT // 2
            for k in range(2):
                done(v.tensor_copy(cs[:, :, half * k:half * k + half],
                                   pb[2 + k][:].rearrange("p (t e) -> p e t", e=E)))
            done(v.tensor_tensor_scan(upto[:].rearrange("p e t -> p (e t)"), ones_l[:].rearrange("p e t -> p (e t)"),
                                      cs[:].rearrange("p e t -> p (e t)"), 0.0, ALU.mult, ALU.add))
            done(v.memset(edge[:, 0:1], 0.0))
            done(v.tensor_copy(edge[:, 1:E + 1], upto[:, :, NT - 1]))
            done(v.tensor_tensor(cnt[:], edge[:, 1:E + 1], edge[:, 0:E], ALU.subtract))
            done(v.tensor_scalar(nblk[:], cnt[:], 1.0 / P, (P - 1.0) / (2 * P), ALU.mult, ALU.add))
            done(v.tensor_scalar(nblk[:], nblk[:], 8388608.0, 8388608.0, ALU.add, ALU.subtract))
            done(v.tensor_tensor_scan(cblk[:], ones_l[:, 0, 0:E], nblk[:], 0.0, ALU.mult, ALU.add))
            done(v.tensor_tensor(base[:], cblk[:], nblk[:], ALU.subtract))
            done(v.scalar_tensor_tensor(base[:], base[:], float(P), edge[:, 0:E], ALU.mult, ALU.subtract))
            done(v.tensor_scalar(clear_f[:, 0:E], rev[0:1], -1.0, float(SPARE + E), ALU.mult, ALU.add))
            done(v.tensor_scalar(has[:], nblk[0:1], 1.0, None, ALU.min))
            done(v.tensor_tensor(last[:], cblk[0:1], clear_f[:, 0:E], ALU.subtract))
            done(v.scalar_tensor_tensor(last[:], last[:], -1.0, has[:], ALU.add, ALU.mult))
            done(v.tensor_tensor(clear_f[:, 0:E], clear_f[:, 0:E], last[:], ALU.add))
            done(v.tensor_copy(clear_f[:, E:E + 1], cblk[0:1, E - 1:E]))
            v.tensor_copy(clear_i[:], clear_f[:]).then_inc(s_clear, 1)
            done(v.tensor_tensor(upto[:], upto[:], cs[:], ALU.subtract))
            done(v.tensor_tensor(upto[:], upto[:], base[:, :, None].to_broadcast([P, E, NT]), ALU.add))
            for k in range(2):
                done(v.tensor_tensor(pos[:, half * k:half * k + half], pb[k][:].rearrange("p (t e) -> p t e", e=E),
                                     upto[:, :, half * k:half * k + half].rearrange("p e t -> p t e"), ALU.add))
            for k in range(TOPK):
                done(v.tensor_tensor(at[:, k], hot[:, k], pos[:], ALU.mult))
                done(v.tensor_reduce(slot_f[:, k], at[:, k], AX.X, ALU.add))
                done(v.tensor_copy(slots[:, :, k], slot_f[:, k]))
            done(v.tensor_tensor(passed[:], cblk[:, None, :].to_broadcast([P, NBT, E]),
                                 blk[:, :, None].to_broadcast([P, NBT, E]), ALU.is_le))
            done(v.tensor_reduce(bcol[:], passed[:], AX.X, ALU.add))
            v.tensor_scalar(bcol[:], bcol[:], float(E - 1), None, ALU.min).then_inc(s_turn, 1)
            ve.wait_ge(s_turn, 2)
            done(v.tensor_copy(bexp[:, 0:NBK], pb[4][0:1, 0:NBK]))
            src = bexp
            for k in range(1, PACK):
                done(v.scalar_tensor_tensor(packed[:], bexp[:, k:k + NBK + PACK], float(1 << (PACK_BITS * k)),
                                            src[:, 0:NBK + PACK], ALU.mult, ALU.add))
                src = packed
            done(v.tensor_copy(block_expert[:], packed[:]))


SHARED_CHUNKS = T // 512 // 2


def load_turned(sp, sems, yt, ynt_d, n, q):
    if not isinstance(n, int) or n > 1:
        sp.wait_ge(sems["yl_ok"], n + 1)
    sp.dma_start(yt[:, q], ynt_d[bass.ds(n * 4, 4)].rearrange("t p c n -> p t c n")).then_inc(sems[f"yt_in{q}"], 16)


class Shared:

    SEMS = "yt_in0 yt_in1 yh_ok yl_ok gu_full sg_ok hf_ok hh_ok hl_ok dn_full so_ok".split()

    def __init__(self, ctx, nc, name, sems, base, split, yt, ynt_d, shgate, so, pb):
        def sb(n, shape, dt=F32):
            return ctx.enter_context(nc.sbuf_tensor(name + n, shape, dt))

        self.nc, self.base, self.ynt_d, self.shgate, self.so, self.pb = nc, base, ynt_d, shgate, so, pb
        self.gh, self.gl, self.dh, self.dl = split
        self.yt = yt
        self.yh = sb("yh", [P, 2, CC, 512], F32R)
        self.yl = sb("yl", [P, 2, CC, 512], F32R)
        self.sg = sb("sg", [P, 2, 512])
        self.hf = sb("hf", [P, 2, 512])
        self.hh = sb("hh", [P, 4, 512], F32R)
        self.hl = sb("hl", [P, 4, 512], F32R)
        self.s = sems

    @staticmethod
    def size(m):
        return P if m < FT - 1 else FL

    @staticmethod
    def chunks(eng, chunk):
        chunk(0, 0, first=True)
        with eng.Fori(0, SHARED_CHUNKS // 2 - 1) as k:
            chunk(k * 2 + 1, 1)
            chunk(k * 2 + 2, 0)
        chunk(SHARED_CHUNKS - 1, 1, last=True)

    def load_yt(self, sp, i, q):
        if not isinstance(i, int) or i > 1:
            load_turned(sp, self.s, self.yt, self.ynt_d, self.base + i, q)

    def split_high(self, act, i, q):
        act.wait_ge(self.s[f"yt_in{q}"], (self.base + i - q) * 8 + 16)
        self.nc.scalar.activation(self.yh[:, q].rearrange("p c (t n) -> p t c n", t=4), self.yt[:, q], ACT.Copy
                                  ).then_inc(self.s["yh_ok"], 1)

    def silu(self, act, i, q, m):
        f, k, g = self.size(m), m % 2, (m + FT * q) % 4
        act.wait_ge(self.s["gu_full"], (self.base + i) * FT + m + 1)
        self.nc.scalar.activation(self.sg[0:f, k], self.pb[2 * k][0:f, :], ACT.Silu).then_inc(self.s["sg_ok"], 1)
        act.wait_ge(self.s["hf_ok"], (self.base + i) * FT + m + 3)
        self.nc.scalar.activation(self.hh[0:f, g], self.hf[0:f, k], ACT.Copy).then_inc(self.s["hh_ok"], 1)

    def leave(self, act, i, q):
        n = self.base + i
        act.wait_ge(self.s["dn_full"], n + 1)
        for t in range(4):
            self.nc.scalar.activation(self.so[:, t:t + 1], self.pb[4 + 2 * q + t // 2][:, None, (t % 2) * C:(t % 2 + 1) * C], ACT.Copy,
                                      scale=self.shgate[:, bass.ds(n * 4 + t, 1)]).then_inc(self.s["so_ok"], 1)

    def credits(self, ve):
        ve.sem_inc(self.s["yl_ok"], 2)
        ve.sem_inc(self.s["hf_ok"], 2)

    def split_low(self, ve, i, q):
        ve.wait_ge(self.s["yh_ok"], self.base + i + 1)
        self.nc.vector.tensor_tensor(self.yl[:, q].rearrange("p c (t n) -> p t c n", t=4), self.yt[:, q],
                                     self.yh[:, q].bitcast(F32).rearrange("p c (t n) -> p t c n", t=4),
                                     ALU.subtract).then_inc(self.s["yl_ok"], 1)

    def gated(self, ve, i, q, m):
        f, k = self.size(m), m % 2
        ve.wait_ge(self.s["sg_ok"], (self.base + i) * FT + m + 1)
        up = self.pb[2 * k + 1][:] if m < FT - 1 else self.pb[2 * k][FL:2 * FL, :]
        self.nc.vector.tensor_tensor(self.hf[0:f, k], self.sg[0:f, k], up, ALU.mult).then_inc(self.s["hf_ok"], 1)

    def hidden_low(self, ve, i, q, m):
        f, k, g = self.size(m), m % 2, (m + FT * q) % 4
        ve.wait_ge(self.s["hh_ok"], (self.base + i) * FT + m + 1)
        self.nc.vector.tensor_tensor(self.hl[0:f, g], self.hf[0:f, k], self.hh[0:f, g].bitcast(F32), ALU.subtract
                                     ).then_inc(self.s["hl_ok"], 1)

    def gate_up(self, pe, i, q, m):
        k = m % 2
        if m == 0:
            pe.wait_ge(self.s["yl_ok"], self.base + i + 3)
        pe.wait_ge(self.s["hf_ok"], (self.base + i) * FT + m + 1)
        for half in range(2 if m < FT - 1 else 1):
            col = (2 * m + half) * P
            j = 0
            for c in range(CC):
                for w, y in ((self.gh, self.yh), (self.gh, self.yl), (self.gl, self.yh)):
                    ins = self.nc.tensor.matmul(self.pb[2 * k + half][:], w[:, c, col:col + P], y[:, q, c, :],
                                                start=(j == 0), stop=(j == 5))
                    j += 1
        ins.then_inc(self.s["gu_full"], 1)

    def down(self, pe, i, q, m):
        g, f = (m + FT * q) % 4, self.size(m)
        pe.wait_ge(self.s["hl_ok"], (self.base + i) * FT + m + 1)
        for t in range(4):
            o = self.pb[4 + 2 * q + t // 2][:, (t % 2) * C:(t % 2 + 1) * C]
            for j, (a, w) in enumerate(((self.hh, self.dh), (self.hh, self.dl), (self.hl, self.dh))):
                ins = self.nc.tensor.matmul(o, a[0:f, g, t * P:(t + 1) * P], w[0:f, m, :],
                                            start=(m == 0 and t % 2 == 0 and j == 0), stop=(m == FT - 1 and j == 2),
                                            skip_group_check=True)
        if m == FT - 1:
            ins.then_inc(self.s["dn_full"], 1)

    def products(self, pe):
        def chunk(i, q, first=False, last=False):
            if first:
                self.gate_up(pe, i, q, 0)
                self.gate_up(pe, i, q, 1)
            for m in range(FT):
                if m + 2 < FT:
                    self.gate_up(pe, i, q, m + 2)
                elif not last:
                    self.gate_up(pe, i + 1, 1 - q, m + 2 - FT)
                self.down(pe, i, q, m)

        self.chunks(pe, chunk)


def shared_and_scatter(nc, sems, we, split, eh, el, yt, ynt_d, yn_d, xg_d, first_d, slots, shgate, sh_d, cleared, pb):
    with ExitStack() as ctx:
        EPC = E // SHARED_CHUNKS
        TPC = NT // SHARED_CHUNKS
        eraw = ctx.enter_context(nc.sbuf_tensor("eraw", [P, EPC, 3 * C], F32))
        yr = ctx.enter_context(nc.sbuf_tensor("yr", [P, TPC // 2, 2, C], F32))
        sl = ctx.enter_context(nc.sbuf_tensor("sl", [P, 2, TPC // 2, 2, TOPK], U32))
        names = "passed e_in0 e_in1 e_hi e_lo yr_in0 yr_in1 yr_in2 yr_in3 sl_ok sc_out0 sc_out1 sc_out2 sc_out3 so_out".split()
        s = {n: ctx.enter_context(nc.semaphore("s_" + n)) for n in names}
        so = ctx.enter_context(nc.sbuf_tensor("sso", [P, 4, C], F32))
        sh = Shared(ctx, nc, "s_", sems, 0, split, yt, ynt_d, shgate, so, pb)
        block = ctx.enter_context(nc.Block())

        @block.sync
        def _(sp):
            def load_yt(i, q):
                sh.load_yt(sp, i, q)

            def load_rows(i, q):
                for t in range(TPC // 2):
                    if not isinstance(i, int) or i > 0:
                        sp.wait_ge(s[f"sc_out{t}"], i * 64)
                    sp.dma_start(yr[:, t], yn_d[bass.ds(i * TPC + 2 * t, 2)].rearrange("t p c -> p t c")
                                 ).then_inc(s[f"yr_in{t}"], 16)

            def load_experts(i, q):
                for k in range(EPC):
                    sp.wait_ge(s["e_lo"], i * EPC + k + 1)
                    sp.dma_start(eraw[:, k:k + 1], we[bass.ds(i * EPC + k, 1)].rearrange("e p w -> p e w")
                                 ).then_inc(s[f"e_in{k}"], 16)

            def store(i, q):
                sp.wait_ge(sems["so_ok"], i * 4 + 4)
                sp.dma_start(sh_d[bass.ds(i * 4, 4)].rearrange("t p c -> p t c"), so[:]).then_inc(s["so_out"], 16)

            sp.dma_start(first_d[30], shgate[:, 0:4]).then_inc(s["so_out"], 16)
            skewed(sp, SHARED_CHUNKS, (2, load_yt), (1, load_rows), (1, load_experts), (-1, store))
            sp.wait_ge(s["so_out"], SHARED_CHUNKS * 16 + 16)

        @block.gpsimd
        def _(po):
            po.wait_ge(cleared, 16 * (E + 1))
            with po.Fori(0, SHARED_CHUNKS // 2) as h:
                for q in range(2):
                    i = h * 2 + q
                    for t in range(TPC // 2):
                        po.wait_ge(s["sl_ok"], i * (TPC // 2) + t + 1)
                        wait_apart(po, s["passed"], s[f"yr_in{t}"], i * 16 + 16)
                        for u in range(2):
                            for k in range(TOPK):
                                nc.gpsimd.indirect_dma_start(
                                    out=xg_d, out_offset=bass.IndirectOffsetOnAxis(ap=sl[:, q, t, u, k:k + 1], axis=0),
                                    in_=yr[:, t, u], in_offset=None).then_inc(s[f"sc_out{t}"], 16)
            for t in range(TPC // 2):
                po.wait_ge(s[f"sc_out{t}"], SHARED_CHUNKS * 64)

        @block.scalar
        def _(act):
            act.preload_act_table(ACT.Silu)

            def chunk(i, q, first=False, last=False):
                if first:
                    sh.split_high(act, i, q)
                for m in range(FT):
                    sh.silu(act, i, q, m)
                    if m == 1 and not first:
                        act.wait_ge(s["so_out"], (i - 1) * 16 + 16)
                        sh.leave(act, i - 1, 1 - q)
                    if m == 2 and not last:
                        sh.split_high(act, i + 1, 1 - q)
                    if m in (3, 4):
                        act.wait_ge(s[f"e_in{m - 3}"], i * 16 + 16)
                        nc.scalar.activation(eh[:, bass.ds(i * EPC + m - 3, 1)], eraw[:, m - 3:m - 2], ACT.Copy).then_inc(s["e_hi"], 1)
                if last:
                    act.wait_ge(s["so_out"], i * 16 + 16)
                    sh.leave(act, i, q)

            sh.chunks(act, chunk)

        @block.vector
        def _(ve):
            sh.credits(ve)
            ve.sem_inc(s["e_lo"], EPC)

            def chunk(i, q, first=False, last=False):
                if first:
                    sh.split_low(ve, i, q)
                for t in range(TPC // 2):
                    if not isinstance(i, int) or i > 1:
                        ve.wait_ge(s[f"sc_out{t}"], (i - 1) * 64)
                    nc.vector.tensor_copy(sl[:, q, t], slots[:, bass.ds(i * TPC + 2 * t, 2), :]).then_inc(s["sl_ok"], 1)
                for m in range(FT):
                    sh.gated(ve, i, q, m)
                    if m == 3 and not last:
                        sh.split_low(ve, i + 1, 1 - q)
                    if m in (4, 5):
                        e = i * EPC + m - 4
                        ve.wait_ge(s["e_hi"], e + 1)
                        nc.vector.tensor_tensor(el[:, bass.ds(e, 1)], eraw[:, m - 4:m - 3], eh[:, bass.ds(e, 1)].bitcast(F32),
                                                ALU.subtract).then_inc(s["e_lo"], 1)
                    sh.hidden_low(ve, i, q, m)

            chunk(0, 0, first=True)
            chunk(1, 1)
            with ve.Fori(0, SHARED_CHUNKS // 2 - 2) as k:
                chunk(k * 2 + 2, 0)
                chunk(k * 2 + 3, 1)
            chunk(SHARED_CHUNKS - 2, 0)
            chunk(SHARED_CHUNKS - 1, 1, last=True)

        @block.tensor
        def _(pe):
            sh.products(pe)


def experts(nc, sems, eh, el, yt, ynt_d, first_d, xg_d, yg_d, ident, ones, block_expert, pb):
    NBK = NBLK + 1
    with ExitStack() as ctx:
        def sb(name, shape, dt=F32):
            return ctx.enter_context(nc.sbuf_tensor(name, shape, dt))

        def sem(name):
            return ctx.enter_context(nc.semaphore(name))

        R = 8
        xg = sb("xg", [P, R, C])
        xh = sb("xh", [P, 2, C], F32R)
        xl = sb("xl", [P, 2, C], F32R)
        sg = sb("esg", [P, 2, P])
        hm = sb("ehm", [P, 2, P])
        hh = sb("ehh", [P, 2, P], F32R)
        hl = sb("ehl", [P, 2, P], F32R)
        yo = sb("yo", [P, R, C])
        names = "x_full xh_ok xl_ok gu_full sg_ok hm_ok ht_full hh_ok hl_ok y_full yo_ok".split()
        s = {n: sem("e_" + n) for n in names}
        xg_in = [sem(f"e_xg_in{k}") for k in range(R)]
        yo_out = [sem(f"e_yo_out{k}") for k in range(R)]
        block = ctx.enter_context(nc.Block())
        px, pg, ph, py = pb[0:2], pb[2:4], pb[4:6], pb[6:8]

        AHEAD = R - 2
        FROM = 1
        TO = FROM + (NBK - AHEAD - FROM) // R * R

        def steps(eng, step, enter=None):
            for n in range(-2, FROM):
                step(n, n % R)
            with eng.Fori(0, (TO - FROM) // R) as i:
                if enter:
                    enter(i * R + FROM, FROM % R)
                for u in range(R):
                    step(i * R + FROM + u, (FROM + u) % R)
            if enter:
                enter(TO, TO % R)
            for n in range(TO, NBK + 1):
                step(n, n % R)

        def parts(n, r, *work):
            for ahead, f in work:
                if not isinstance(n, int) or 0 <= n + ahead < NBK:
                    f(n + ahead, (r + ahead) % R)

        @block.sync
        def _(sp):
            def load(b, r):
                sp.wait_ge(s["x_full"], b + 1)
                sp.dma_start(xg[:, r], xg_d[bass.ds(b * P, P)] if not isinstance(b, int) else xg_d[b * P:b * P + P]
                             ).then_inc(xg_in[r], 16)

            def store(b, r):
                sp.wait_ge(s["yo_ok"], b + 3)
                sp.dma_start(yg_d[bass.ds(b * P, P)] if not isinstance(b, int) else yg_d[b * P:b * P + P], yo[:, r]
                             ).then_inc(yo_out[r], 16)

            for b in range(AHEAD - 2):
                load(b, b)
            for k in range(R):
                sp.dma_start(first_d[17 + k], ones[:, 0:4]).then_inc(yo_out[k], 16)
            for q in range(2):
                load_turned(sp, sems, yt, ynt_d, SHARED_CHUNKS + q, q)
            steps(sp, lambda n, r: parts(n, r, (AHEAD, load), (-1, store)))
            for k in range(R):
                sp.wait_ge(yo_out[k], 16 + NBK // R * 16)

        @block.tensor
        def _(pe):
            pe.sem_inc(s["x_full"], R)
            def turn_x(b, r):
                pe.wait_ge(xg_in[r], (b - r) * (16 // R) + 16)
                for c in range(CC):
                    ins = nc.tensor.transpose(px[r % 2][:, c * P:(c + 1) * P], xg[:, r, c * P:(c + 1) * P], ident[:])
                ins.then_inc(s["x_full"], 1)

            held, words = {}, []

            def load_words(b):
                words.clear()
                for k in range(2):
                    at = block_expert[0:1, bass.ds(b + PACK * k, 1)]
                    w = pe.value_load(at, min_val=0, max_val=(1 << (PACK_BITS * PACK)) - 1)
                    words.extend((w, PACK_BITS * j) for j in range(PACK))

            def find(_, r):
                if words:
                    w, shift = words.pop(0)
                    held[r] = (w >> shift) & (E - 1)

            def enter(n, r):
                load_words(n - 1)
                for k in range(-1, 2):
                    find(n + k, (r + k) % R)

            def gate_up(b, r):
                e = held[r]
                pe.wait_ge(s["xl_ok"], b + 3)
                j = 0
                for c in range(CC):
                    for a, w in ((xh, eh), (xh, el), (xl, eh)):
                        ins = nc.tensor.matmul(pg[r % 2][:, 0:2 * MF], a[:, r % 2, c * P:(c + 1) * P],
                                               w[:, bass.ds(e, 1), c * C:(c + 1) * C], start=(j == 0), stop=(j == 5))
                        j += 1
                ins.then_inc(s["gu_full"], 1)

            def turn_h(b, r):
                pe.wait_ge(s["hm_ok"], b + 3)
                nc.tensor.transpose(ph[r % 2][:, 0:P], hm[:, r % 2], ident[:]).then_inc(s["ht_full"], 1)

            def down(b, r):
                e = held[r]
                pe.wait_ge(s["hl_ok"], b + 3)
                pe.wait_ge(s["yo_ok"], b + 1)
                for j, (a, w) in enumerate(((hh, eh), (hh, el), (hl, eh))):
                    ins = nc.tensor.matmul(py[r % 2][:, 0:C], a[:, r % 2], w[:, bass.ds(e, 1), 2 * C:3 * C],
                                           start=(j == 0), stop=(j == 2))
                ins.then_inc(s["y_full"], 1)

            load_words(0)
            steps(pe, lambda n, r: parts(n, r, (2, turn_x), (1, gate_up), (0, turn_h), (-1, down), (2, find)), enter)

        @block.scalar
        def _(act):
            act.preload_act_table(ACT.Silu)

            def x_high(b, r):
                act.wait_ge(s["x_full"], b + 1 + R)
                nc.scalar.activation(xh[:, r % 2], px[r % 2][:, 0:C], ACT.Copy).then_inc(s["xh_ok"], 1)

            def silu(b, r):
                act.wait_ge(s["gu_full"], b + 1)
                nc.scalar.activation(sg[:, r % 2], pg[r % 2][:, 0:MF], ACT.Silu).then_inc(s["sg_ok"], 1)

            def h_high(b, r):
                act.wait_ge(s["ht_full"], b + 1)
                nc.scalar.activation(hh[:, r % 2], ph[r % 2][:, 0:P], ACT.Copy).then_inc(s["hh_ok"], 1)

            steps(act, lambda n, r: parts(n, r, (2, x_high), (1, silu), (0, h_high)))

        @block.vector
        def _(ve):
            for name in ("xl_ok", "hm_ok", "hl_ok", "yo_ok"):
                ve.sem_inc(s[name], 2)

            def x_low(b, r):
                ve.wait_ge(s["xh_ok"], b + 1)
                nc.vector.tensor_tensor(xl[:, r % 2], px[r % 2][:, 0:C], xh[:, r % 2].bitcast(F32), ALU.subtract).then_inc(s["xl_ok"], 1)

            def gated(b, r):
                ve.wait_ge(s["sg_ok"], b + 1)
                nc.vector.tensor_tensor(hm[:, r % 2], sg[:, r % 2], pg[r % 2][:, MF:2 * MF], ALU.mult).then_inc(s["hm_ok"], 1)

            def h_low(b, r):
                ve.wait_ge(s["hh_ok"], b + 1)
                nc.vector.tensor_tensor(hl[:, r % 2], ph[r % 2][:, 0:P], hh[:, r % 2].bitcast(F32), ALU.subtract).then_inc(s["hl_ok"], 1)

            def leave(b, r):
                ve.wait_ge(s["y_full"], b + 1)
                ve.wait_ge(yo_out[r], (b - r) * (16 // R) + 16)
                nc.vector.tensor_copy(yo[:, r], py[r % 2][:, 0:C]).then_inc(s["yo_ok"], 1)

            steps(ve, lambda n, r: parts(n, r, (2, x_low), (1, gated), (0, h_low), (-1, leave)))


def shared_and_combine(nc, sems, split, yt, first_d, ynt_d, x2_d, yg_d, sh_d, ones, neg_half, eps, slots, share, shgate, out, pb):
    out_t = out.rearrange("a (n p) c -> (a n) p c", p=P)
    G = 4
    with ExitStack() as ctx:
        def sb(name, shape, dt=F32):
            return ctx.enter_context(nc.sbuf_tensor(name, shape, dt))

        so = sb("cso", [P, G, C])
        kept = sb("ckept", [P, G, C])
        y = sb("cy", [P, 2, G, TOPK, C])
        x2 = sb("cx2", [P, 2, G, C])
        ff = sb("cff", [P, 2, G, C])
        o = sb("co", [P, 2, G, C])
        sl = sb("csl", [P, 2, G, TOPK], U32)
        st = sb("cst", [P, 2, G, 6])
        mv = sb("cmv", [P, 2, G, 2])
        rstd = sb("crstd", [P, 2, G])
        shift = sb("cshift", [P, 2, G])
        zero = sb("czero", [P, G])
        names = ["passed", "vpassed", "zeros", "kept_in"] + [f"{n}{v}" for v in range(2) for n in
                 "sl_ok y_in x2_in s1_ok s2_ok st_ok mv_ok var_ok dev_ok norm_ok z_ok o_ok o_out".split()]
        s = {n: ctx.enter_context(nc.semaphore("c_" + n)) for n in names}
        sh = Shared(ctx, nc, "c_", sems, SHARED_CHUNKS, split, yt, ynt_d, shgate, so, pb)
        block = ctx.enter_context(nc.Block())

        def first_tile(v, i):
            return i * G + v * (NT // 2)

        @block.sync
        def _(sp):
            for v in range(2):
                sp.dma_start(first_d[8 + v], ones[:, 0:4]).then_inc(s[f"o_out{v}"], 16)

            def load_yt(i, q):
                sh.load_yt(sp, i, q)

            def load_x2(v):
                def f(i, q):
                    sp.wait_ge(s[f"o_ok{v}"], i * G + G)
                    sp.dma_start(x2[:, v], x2_d[bass.ds(first_tile(v, i), G)].rearrange("t p c -> p t c")
                                 ).then_inc(s[f"x2_in{v}"], 16)
                return f

            def load_kept(i, q):
                if not isinstance(i, int) or i > 0:
                    sp.wait_ge(s["s1_ok0"], i * G)
                sp.dma_start(kept[:], sh_d[bass.ds(i * G, G)].rearrange("t p c -> p t c")).then_inc(s["kept_in"], 16)

            def store(v):
                def f(i, q):
                    sp.wait_ge(s[f"o_ok{v}"], i * G + 2 * G)
                    sp.dma_start(out_t[bass.ds(first_tile(v, i), G)].rearrange("t p c -> p t c"), o[:, v]
                                 ).then_inc(s[f"o_out{v}"], 16)
                return f

            skewed(sp, SHARED_CHUNKS, (2, load_yt), (0, load_kept), (-2, store(1)), (-1, load_x2(1)), (-1, store(0)), (0, load_x2(0)))
            for v in range(2):
                sp.wait_ge(s[f"o_out{v}"], 16 + SHARED_CHUNKS * 16)

        @block.gpsimd
        def _(po):
            nc.gpsimd.memset(zero[:], 0.0).then_inc(s["zeros"], 1)
            po.wait_ge(s["zeros"], 1)

            def gather(v, i):
                wait_apart(po, s["passed"], s[f"sl_ok{v}"], i + 1)
                for k in range(G):
                    for j in range(TOPK):
                        nc.gpsimd.indirect_dma_start(out=y[:, v, k, j], out_offset=None, in_=yg_d,
                                                     in_offset=bass.IndirectOffsetOnAxis(ap=sl[:, v, k, j:j + 1], axis=0)
                                                     ).then_inc(s[f"y_in{v}"], 16)

            def scales(v, i):
                po.wait_ge(s[f"mv_ok{v}"], i * G + G)
                for k in range(0, G, 2):
                    nc.gpsimd.tensor_tensor(rstd[:, v, k:k + 2], mv[:, v, k:k + 2, 1], eps[:, 0:2], ALU.add).then_inc(s[f"var_ok{v}"], 1)
                nc.gpsimd.tensor_tensor(shift[:, v], zero[:], mv[:, v, :, 0], ALU.subtract).then_inc(s[f"var_ok{v}"], 1)
                po.wait_ge(s[f"var_ok{v}"], i * 3 + 3)
                for k in range(0, G, 2):
                    nc.gpsimd.tensor_tensor(rstd[:, v, k:k + 2], rstd[:, v, k:k + 2], neg_half[:, 0:2], ALU.pow).then_inc(s[f"dev_ok{v}"], 1)
                po.wait_ge(s[f"dev_ok{v}"], i * 2 + 2)
                nc.gpsimd.tensor_tensor(shift[:, v], shift[:, v], rstd[:, v], ALU.mult).then_inc(s[f"norm_ok{v}"], 1)

            gather(0, 0)
            gather(1, 0)
            with po.Fori(0, SHARED_CHUNKS - 1) as i:
                scales(0, i)
                gather(0, i + 1)
                scales(1, i)
                gather(1, i + 1)
            scales(0, SHARED_CHUNKS - 1)
            scales(1, SHARED_CHUNKS - 1)

        @block.scalar
        def _(act):
            act.preload_act_table(ACT.Silu)

            def centred(v, i):
                act.wait_ge(s[f"norm_ok{v}"], i + 1)
                for k in range(G):
                    nc.scalar.activation(ff[:, v, k], ff[:, v, k], ACT.Identity, scale=rstd[:, v, k:k + 1],
                                         bias=shift[:, v, k:k + 1]).then_inc(s[f"z_ok{v}"], 1)

            def chunk(i, q, first=False, last=False):
                if first:
                    sh.split_high(act, i, q)
                for m in range(FT):
                    sh.silu(act, i, q, m)
                    if m == 0 and not first:
                        sh.leave(act, i - 1, 1 - q)
                    if m == 1 and not last:
                        sh.split_high(act, i + 1, 1 - q)
                    if m == 2 and not first:
                        centred(0, i - 1)
                    if m == FT - 1 and not first:
                        centred(1, i - 1)
                if last:
                    centred(0, i)
                    sh.leave(act, i, q)
                    centred(1, i)

            sh.chunks(act, chunk)

        @block.vector
        def _(ve):
            for v in range(2):
                ve.sem_inc(s[f"o_ok{v}"], G)

            def find(v, i):
                nc.vector.tensor_copy(sl[:, v], slots[:, bass.ds(first_tile(v, i), G), :]).then_inc(s[f"sl_ok{v}"], 1)

            def sums(v, i, tiles):
                def each():
                    return ((k, first_tile(v, i) + k, i * G + k) for k in tiles)

                if 0 in tiles:
                    ve.wait_ge(s[f"y_in{v}"], (i + 1) * (16 * G * TOPK))
                    if v == 0:
                        ve.wait_ge(s["kept_in"], i * 16 + 16)
                for k, m, c in each():
                    ve.wait_ge(s[f"o_ok{v}"], c + 1)
                    if v == 1:
                        ve.wait_ge(sems["so_ok"], NT // 2 + c + 1)
                    nc.vector.scalar_tensor_tensor(ff[:, v, k:k + 1], y[:, v, k, 0:1], share[:, bass.ds(m, 1), 0],
                                                   (so if v else kept)[:, k:k + 1], ALU.mult, ALU.add).then_inc(s[f"s1_ok{v}"], 1)
                for k, m, c in each():
                    ve.wait_ge(s[f"s1_ok{v}"], c + 1)
                    nc.vector.scalar_tensor_tensor(ff[:, v, k], y[:, v, k, 1], share[:, bass.ds(m, 1), 1], ff[:, v, k],
                                                   ALU.mult, ALU.add).then_inc(s[f"s2_ok{v}"], 1)
                for k, m, c in each():
                    ve.wait_ge(s[f"s2_ok{v}"], c + 1)
                    nc.vector.bn_stats(st[:, v, k], ff[:, v, k]).then_inc(s[f"st_ok{v}"], 1)
                for k, m, c in each():
                    wait_apart(ve, s["vpassed"], s[f"st_ok{v}"], c + 1)
                    nc.vector.bn_aggr(mv[:, v, k], st[:, v, k]).then_inc(s[f"mv_ok{v}"], 1)

            def finish(v, i):
                ve.wait_ge(s[f"x2_in{v}"], i * 16 + 16)
                ve.wait_ge(s[f"o_out{v}"], i * 16 + 16)
                for k in range(G):
                    ve.wait_ge(s[f"z_ok{v}"], i * G + k + 1)
                    nc.vector.tensor_tensor(o[:, v, k], ff[:, v, k], x2[:, v, k], ALU.add).then_inc(s[f"o_ok{v}"], 1)

            def chunk(i, q, first=False, last=False):
                if first:
                    find(0, 0)
                    find(1, 0)
                    sh.split_low(ve, i, q)
                for m in range(FT):
                    sh.gated(ve, i, q, m)
                    if m == 0 and not first and not (isinstance(i, int) and i < 2):
                        finish(1, i - 2)
                    if m == 1 and not first:
                        sums(1, i - 1, (0, 1))
                    if m == 2 and not first:
                        sums(1, i - 1, (2, 3))
                        find(1, i)
                    if m == 3 and not first:
                        finish(0, i - 1)
                    if m == 3 and not last:
                        sh.split_low(ve, i + 1, 1 - q)
                    if m == 4:
                        sums(0, i, (0, 1))
                    if m == 5:
                        sums(0, i, (2, 3))
                        if not last:
                            find(0, i + 1)
                    sh.hidden_low(ve, i, q, m)
                if last:
                    finish(1, i - 1)
                    finish(0, i)
                    sums(1, i, range(G))
                    finish(1, i)

            chunk(0, 0, first=True)
            chunk(1, 1)
            with ve.Fori(0, SHARED_CHUNKS // 2 - 2) as k:
                chunk(k * 2 + 2, 0)
                chunk(k * 2 + 3, 1)
            chunk(SHARED_CHUNKS - 2, 0)
            chunk(SHARED_CHUNKS - 1, 1, last=True)

        @block.tensor
        def _(pe):
            sh.products(pe)


def _layouts(i):
    import numpy as np

    taps = i["L0_attn_w_lin"].reshape(HEADS, KS, C)
    ring = np.concatenate([taps, taps[:, KS - 1:]], 1)[:, [(k - 1) % J for k in range(2 * J)]]
    wd = ring.transpose(2, 0, 1).reshape(CC, P, HEADS, 2 * J).transpose(1, 0, 2, 3)
    g = np.concatenate([i["L0_ffn_gate_w"], i["L0_ffn_shared_gate_w"], np.zeros((GW - E - 1, C), "f")], 0)
    gw = g.T.reshape(CC, P, GW).transpose(1, 0, 2)
    gate, up = i["L0_ffn_shared_w_gate"], i["L0_ffn_shared_w_up"]
    rows = [a[m * P:(m + 1) * P] for m in range(FT) for a in (gate, up)]
    wsh = np.concatenate(rows, 0).T.reshape(CC, P, 2 * FF).transpose(1, 0, 2)
    dn = np.concatenate([i["L0_ffn_shared_w_down"].T, np.zeros((FT * P - FF, C), "f")], 0)
    wdn = dn.reshape(FT, P, C).transpose(1, 0, 2)
    gu = i["L0_ffn_w_gate_up"].reshape(E, CC, P, 2 * MF).transpose(0, 2, 1, 3).reshape(E, P, CC * 2 * MF)
    we = np.concatenate([gu, i["L0_ffn_w_down"]], 2)
    named = dict(x=i["L0_attn_x"], wd=wd, gw=gw, wsh=wsh, wdn=wdn, we=we)
    return {k: np.ascontiguousarray(v) for k, v in named.items()}


def kernel(**inputs):
    import numpy as np
    import concourse.bacc as bacc
    from concourse.bass_utils import run_bass_kernel_spmd

    arrays = _layouts({k: np.asarray(v) for k, v in inputs.items()})
    nc = bacc.Bacc("TRN2", target_bir_lowering=False, num_devices=1)
    args = [nc.dram_tensor(n, a.shape, mybir.dt.from_np(a.dtype), kind="ExternalInput").ap() for n, a in arrays.items()]
    out = nc.dram_tensor("out", (BATCH, SEQ, C), F32, kind="ExternalOutput").ap()
    build_program(nc, *args, out)
    result = run_bass_kernel_spmd(nc, [arrays], core_ids=[0])
    return result.results[0]["out"]
```
